# Optimizing a Trainium2 kernel written in Bass

```python
import numpy as np
import jax
import jax.numpy as jnp

def _softmax(x, axis=-1):
    return jax.nn.softmax(x, axis=axis)

def _gelu(x):
    return jax.nn.gelu(x, approximate=True)

def _silu(x):
    return jax.nn.silu(x)

def _sigmoid(x):
    return jax.nn.sigmoid(x)

def _layernorm(x, axis=-1, eps=1e-05):
    m = jnp.mean(x, axis=axis, keepdims=True)
    v = jnp.var(x, axis=axis, keepdims=True)
    return (x - m) / jnp.sqrt(v + eps)

def _scatter_add(tgt, idx, src, axis=0):
    return tgt.at[idx].add(src)

def _segment_sum(src, seg, n):
    return jax.ops.segment_sum(src, seg, n)
kernel_name = 'mk_adaln_d1_jaxref_r8_86285e'

def setup_inputs(seed: int=0):
    np.random.seed(seed)
    _w = jnp.asarray

    def _L0_attn_setup():
        import jax, jax.numpy as jnp
        import numpy as np
        B, L, D, E, N, DDELTA, DCONV = (4, 256, 128, 256, 16, 64, 4)
        EPS = 1e-05
        key = jax.random.key(seed)
        ks = jax.random.split(key, 12)

        def rn(k, shape, scale=0.02):
            return (jax.random.normal(k, shape) * scale).astype(jnp.float32)
        return {'resid': jax.random.normal(ks[0], (B, L, D), dtype=jnp.float32), 'norm_w': jnp.ones((D,), jnp.float32), 'skip_w': rn(ks[1], (E, D)), 'in_w': rn(ks[2], (E, D)), 'conv_w': rn(ks[3], (E, 1, DCONV), 0.1), 'conv_b': jnp.zeros((E,), jnp.float32), 'Wd1': rn(ks[4], (DDELTA, E)), 'Wd2_w': rn(ks[5], (E, DDELTA)), 'Wd2_b': rn(ks[6], (E,), 0.01), 'WB': rn(ks[7], (N, E)), 'WC': rn(ks[8], (N, E)), 'A_log': (jax.random.normal(ks[9], (E, N)) * 0.5).astype(jnp.float32), 'W_D': jnp.ones((E,), jnp.float32), 'out_w': rn(ks[10], (D, E))}
    _L0_attn_in = _L0_attn_setup()

    def _L0_ffn_setup():
        import jax, jax.numpy as jnp
        import numpy as np
        DIM = 128
        DEPTH = 6
        HEADS = 16
        DIM_HEAD = 64
        WINDOW = 32
        INNER = HEADS * DIM_HEAD
        DIM_INNER = int(DIM * 4 * 2 / 3)
        QK_SCALE = 8.0

        def shift_tokens(t):
            a, s = jnp.split(t, 2, -1)
            s = jnp.pad(s, ((0, 0), (1, 0), (0, 0)))[:, :-1]
            return jnp.concatenate([a, s], -1)

        def l2norm(t):
            return t / jnp.maximum(jnp.linalg.norm(t, axis=-1, keepdims=True), 1e-12)

        def rotate_half(x):
            x1, x2 = jnp.split(x, 2, -1)
            return jnp.concatenate([-x2, x1], -1)

        def rotary_tables(n):
            half = jnp.arange(0, DIM_HEAD, 2, dtype=jnp.float32)
            inv_freq = 1.0 / 10000.0 ** (half / DIM_HEAD)
            t = jnp.arange(n, dtype=jnp.float32)
            freqs = t[:, None] * inv_freq[None, :]
            freqs = jnp.concatenate([freqs, freqs], -1)
            base_scale = (half + 0.4 * DIM_HEAD) / (1.4 * DIM_HEAD)
            power = (t - n // 2) / (WINDOW // 2)
            scale = base_scale[None, :] ** power[:, None]
            scale = jnp.concatenate([scale, scale], -1)
            return (freqs, scale)

        def local_attention(q, k, v):
            b, h, n, d = q.shape
            w = WINDOW
            nw = n // w
            bq = q.reshape(b, h, nw, w, d)
            bk = k.reshape(b, h, nw, w, d)
            bv = v.reshape(b, h, nw, w, d)

            def look(t):
                p = jnp.pad(t, ((0, 0), (0, 0), (1, 0), (0, 0), (0, 0)))
                return jnp.concatenate([p[:, :, :nw], p[:, :, 1:]], axis=3)
            bk2, bv2 = (look(bk), look(bv))
            seq = jnp.arange(n).reshape(nw, w)
            seq_p = jnp.pad(seq, ((1, 0), (0, 0)), constant_values=-1)
            jt = jnp.concatenate([seq_p[:nw], seq_p[1:]], axis=1)
            it = seq[:, :, None]
            jb = jt[:, None, :]
            mask = (it < jb) | (it > jb + w) | (jb == -1)
            sim = jnp.einsum('bhwie,bhwje->bhwij', bq, bk2) * QK_SCALE
            sim = jnp.where(mask, -jnp.finfo(sim.dtype).max, sim)
            attn = jax.nn.softmax(sim, -1)
            out = jnp.einsum('bhwij,bhwje->bhwie', attn, bv2)
            return out.reshape(b, h, n, d)

        def attn_layer(x, Wqkv, qs, ksc, Wo):
            b, n, _ = x.shape
            qkv = x @ Wqkv
            q, k, v = jnp.split(qkv, 3, -1)
            sh = lambda t: t.reshape(b, n, HEADS, DIM_HEAD).transpose(0, 2, 1, 3)
            q, k, v = (sh(q), sh(k), sh(v))
            q = l2norm(q) * qs
            k = l2norm(k) * ksc
            freqs, scale = rotary_tables(n)
            cos, sin = (jnp.cos(freqs), jnp.sin(freqs))
            q = q * cos * scale + rotate_half(q) * sin * scale
            inv = 1.0 / scale
            k = k * cos * inv + rotate_half(k) * sin * inv
            out = local_attention(q, k, v)
            out = out.transpose(0, 2, 1, 3).reshape(b, n, INNER)
            return out @ Wo

        def ffn_layer(x, g, bln, W1, b1, W2, b2):
            mu = x.mean(-1, keepdims=True)
            var = ((x - mu) ** 2).mean(-1, keepdims=True)
            xn = (x - mu) / jnp.sqrt(var + 1e-05) * g + bln
            hg = xn @ W1 + b1
            a, gate = jnp.split(hg, 2, -1)
            return a * jax.nn.gelu(gate, approximate=False) @ W2 + b2
        key = jax.random.key(seed)
        ks = jax.random.split(key, 8)
        B, N = (2, 256)
        init = lambda k, shape: jax.random.normal(k, shape, jnp.float32) * 0.02
        return {'x': jax.random.normal(ks[0], (B, N, DIM), jnp.float32), 'Wqkv': init(ks[1], (DEPTH, DIM, 3 * INNER)), 'q_scale': jnp.ones((DEPTH, DIM_HEAD), jnp.float32), 'k_scale': jnp.ones((DEPTH, DIM_HEAD), jnp.float32), 'Wo': init(ks[2], (DEPTH, INNER, DIM)), 'ln_g': jnp.ones((DEPTH, DIM), jnp.float32), 'ln_b': jnp.zeros((DEPTH, DIM), jnp.float32), 'W1': init(ks[3], (DEPTH, DIM, 2 * DIM_INNER)), 'b1': jnp.zeros((DEPTH, 2 * DIM_INNER), jnp.float32), 'W2': init(ks[4], (DEPTH, DIM_INNER, DIM)), 'b2': jnp.zeros((DEPTH, DIM), jnp.float32)}
    _L0_ffn_in = _L0_ffn_setup()
    _L0_c = _w((lambda *s: np.random.randn(*s).astype(np.float32) * 0.05)(2, 128))
    _L0_wmod = _w((lambda *s: np.random.randn(*s).astype(np.float32) * 0.05)(128, 6 * 128) * 128 ** (-0.5))
    _d = {'L0_attn_resid': _L0_attn_in['resid'], 'L0_attn_norm_w': _L0_attn_in['norm_w'], 'L0_attn_skip_w': _L0_attn_in['skip_w'], 'L0_attn_in_w': _L0_attn_in['in_w'], 'L0_attn_conv_w': _L0_attn_in['conv_w'], 'L0_attn_conv_b': _L0_attn_in['conv_b'], 'L0_attn_Wd1': _L0_attn_in['Wd1'], 'L0_attn_Wd2_w': _L0_attn_in['Wd2_w'], 'L0_attn_Wd2_b': _L0_attn_in['Wd2_b'], 'L0_attn_WB': _L0_attn_in['WB'], 'L0_attn_WC': _L0_attn_in['WC'], 'L0_attn_A_log': _L0_attn_in['A_log'], 'L0_attn_W_D': _L0_attn_in['W_D'], 'L0_attn_out_w': _L0_attn_in['out_w'], 'L0_ffn_Wqkv': _L0_ffn_in['Wqkv'], 'L0_ffn_q_scale': _L0_ffn_in['q_scale'], 'L0_ffn_k_scale': _L0_ffn_in['k_scale'], 'L0_ffn_Wo': _L0_ffn_in['Wo'], 'L0_ffn_ln_g': _L0_ffn_in['ln_g'], 'L0_ffn_ln_b': _L0_ffn_in['ln_b'], 'L0_ffn_W1': _L0_ffn_in['W1'], 'L0_ffn_b1': _L0_ffn_in['b1'], 'L0_ffn_W2': _L0_ffn_in['W2'], 'L0_ffn_b2': _L0_ffn_in['b2'], 'L0_c': _L0_c, 'L0_wmod': _L0_wmod}
    _x0 = _d['L0_attn_resid']
    _d['L0_attn_resid'] = jax.random.normal(jax.random.fold_in(jax.random.key(seed), 1), (2, 1024, 128), dtype=_x0.dtype)
    del _x0
    return _d

def reference(L0_attn_resid, L0_attn_norm_w, L0_attn_skip_w, L0_attn_in_w, L0_attn_conv_w, L0_attn_conv_b, L0_attn_Wd1, L0_attn_Wd2_w, L0_attn_Wd2_b, L0_attn_WB, L0_attn_WC, L0_attn_A_log, L0_attn_W_D, L0_attn_out_w, L0_ffn_Wqkv, L0_ffn_q_scale, L0_ffn_k_scale, L0_ffn_Wo, L0_ffn_ln_g, L0_ffn_ln_b, L0_ffn_W1, L0_ffn_b1, L0_ffn_W2, L0_ffn_b2, L0_c, L0_wmod):

    def _L0_attn_ref(resid, norm_w, skip_w, in_w, conv_w, conv_b, Wd1, Wd2_w, Wd2_b, WB, WC, A_log, W_D, out_w):
        import jax, jax.numpy as jnp
        import numpy as np
        B, L, D, E, N, DDELTA, DCONV = (4, 256, 128, 256, 16, 64, 4)
        EPS = 1e-05
        x = resid * jax.lax.rsqrt(jnp.mean(resid * resid, axis=-1, keepdims=True) + EPS) * norm_w
        skip = x @ skip_w.T
        x = x @ in_w.T
        xc = jnp.transpose(x, (0, 2, 1))
        xc = jax.lax.conv_general_dilated(xc, conv_w, window_strides=(1,), padding=[(DCONV - 1, 0)], dimension_numbers=('NCH', 'OIH', 'NCH'), feature_group_count=conv_w.shape[0])
        x = jnp.transpose(xc, (0, 2, 1)) + conv_b
        x = jax.nn.silu(x)
        A = -jnp.exp(A_log)
        delta = jax.nn.softplus(x @ Wd1.T @ Wd2_w.T + Wd2_b)
        Bm = x @ WB.T
        Cm = x @ WC.T

        def step(h, inp):
            x_l, d_l, B_l, C_l = inp
            A_bar = jnp.exp(d_l[:, :, None] * A)
            h = A_bar * h + (d_l * x_l)[:, :, None] * B_l[:, None, :]
            y_l = jnp.einsum('ben,bn->be', h, C_l)
            return (h, y_l)
        h0 = jnp.zeros((resid.shape[0], A.shape[0], A.shape[1]), x.dtype)
        xs = (jnp.swapaxes(x, 0, 1), jnp.swapaxes(delta, 0, 1), jnp.swapaxes(Bm, 0, 1), jnp.swapaxes(Cm, 0, 1))
        _, ys = jax.lax.scan(step, h0, xs)
        y = jnp.swapaxes(ys, 0, 1)
        y = y + x * W_D
        y = y * jax.nn.silu(skip)
        y = y @ out_w.T
        return resid + y

    def _L0_ffn_ref(x, Wqkv, q_scale, k_scale, Wo, ln_g, ln_b, W1, b1, W2, b2):
        import jax, jax.numpy as jnp
        import numpy as np
        DIM = 128
        DEPTH = 6
        HEADS = 16
        DIM_HEAD = 64
        WINDOW = 32
        INNER = HEADS * DIM_HEAD
        DIM_INNER = int(DIM * 4 * 2 / 3)
        QK_SCALE = 8.0

        def shift_tokens(t):
            a, s = jnp.split(t, 2, -1)
            s = jnp.pad(s, ((0, 0), (1, 0), (0, 0)))[:, :-1]
            return jnp.concatenate([a, s], -1)

        def l2norm(t):
            return t / jnp.maximum(jnp.linalg.norm(t, axis=-1, keepdims=True), 1e-12)

        def rotate_half(x):
            x1, x2 = jnp.split(x, 2, -1)
            return jnp.concatenate([-x2, x1], -1)

        def rotary_tables(n):
            half = jnp.arange(0, DIM_HEAD, 2, dtype=jnp.float32)
            inv_freq = 1.0 / 10000.0 ** (half / DIM_HEAD)
            t = jnp.arange(n, dtype=jnp.float32)
            freqs = t[:, None] * inv_freq[None, :]
            freqs = jnp.concatenate([freqs, freqs], -1)
            base_scale = (half + 0.4 * DIM_HEAD) / (1.4 * DIM_HEAD)
            power = (t - n // 2) / (WINDOW // 2)
            scale = base_scale[None, :] ** power[:, None]
            scale = jnp.concatenate([scale, scale], -1)
            return (freqs, scale)

        def local_attention(q, k, v):
            b, h, n, d = q.shape
            w = WINDOW
            nw = n // w
            bq = q.reshape(b, h, nw, w, d)
            bk = k.reshape(b, h, nw, w, d)
            bv = v.reshape(b, h, nw, w, d)

            def look(t):
                p = jnp.pad(t, ((0, 0), (0, 0), (1, 0), (0, 0), (0, 0)))
                return jnp.concatenate([p[:, :, :nw], p[:, :, 1:]], axis=3)
            bk2, bv2 = (look(bk), look(bv))
            seq = jnp.arange(n).reshape(nw, w)
            seq_p = jnp.pad(seq, ((1, 0), (0, 0)), constant_values=-1)
            jt = jnp.concatenate([seq_p[:nw], seq_p[1:]], axis=1)
            it = seq[:, :, None]
            jb = jt[:, None, :]
            mask = (it < jb) | (it > jb + w) | (jb == -1)
            sim = jnp.einsum('bhwie,bhwje->bhwij', bq, bk2) * QK_SCALE
            sim = jnp.where(mask, -jnp.finfo(sim.dtype).max, sim)
            attn = jax.nn.softmax(sim, -1)
            out = jnp.einsum('bhwij,bhwje->bhwie', attn, bv2)
            return out.reshape(b, h, n, d)

        def attn_layer(x, Wqkv, qs, ksc, Wo):
            b, n, _ = x.shape
            qkv = x @ Wqkv
            q, k, v = jnp.split(qkv, 3, -1)
            sh = lambda t: t.reshape(b, n, HEADS, DIM_HEAD).transpose(0, 2, 1, 3)
            q, k, v = (sh(q), sh(k), sh(v))
            q = l2norm(q) * qs
            k = l2norm(k) * ksc
            freqs, scale = rotary_tables(n)
            cos, sin = (jnp.cos(freqs), jnp.sin(freqs))
            q = q * cos * scale + rotate_half(q) * sin * scale
            inv = 1.0 / scale
            k = k * cos * inv + rotate_half(k) * sin * inv
            out = local_attention(q, k, v)
            out = out.transpose(0, 2, 1, 3).reshape(b, n, INNER)
            return out @ Wo

        def ffn_layer(x, g, bln, W1, b1, W2, b2):
            mu = x.mean(-1, keepdims=True)
            var = ((x - mu) ** 2).mean(-1, keepdims=True)
            xn = (x - mu) / jnp.sqrt(var + 1e-05) * g + bln
            hg = xn @ W1 + b1
            a, gate = jnp.split(hg, 2, -1)
            return a * jax.nn.gelu(gate, approximate=False) @ W2 + b2
        for i in range(DEPTH):
            x = attn_layer(shift_tokens(x), Wqkv[i], q_scale[i], k_scale[i], Wo[i]) + x
            x = ffn_layer(shift_tokens(x), ln_g[i], ln_b[i], W1[i], b1[i], W2[i], b2[i]) + x
        return x
    x = L0_attn_resid
    mod = (_silu(L0_c) @ L0_wmod).reshape(L0_c.shape[0], 6, 1, -1)
    sa, ca, ga, sb, cb, gb = (mod[:, 0], mod[:, 1], mod[:, 2], mod[:, 3], mod[:, 4], mod[:, 5])
    ga = (2 * (ga >= 0) - 1) * jnp.maximum(jnp.abs(ga), 0.25)
    gb = (2 * (gb >= 0) - 1) * jnp.maximum(jnp.abs(gb), 0.25)
    h = _layernorm(x, axis=-1) * (1 + ca) + sa
    x = x + ga * _L0_attn_ref(h, L0_attn_norm_w, L0_attn_skip_w, L0_attn_in_w, L0_attn_conv_w, L0_attn_conv_b, L0_attn_Wd1, L0_attn_Wd2_w, L0_attn_Wd2_b, L0_attn_WB, L0_attn_WC, L0_attn_A_log, L0_attn_W_D, L0_attn_out_w)
    h = _layernorm(x, axis=-1) * (1 + cb) + sb
    x = x + gb * _L0_ffn_ref(h, L0_ffn_Wqkv, L0_ffn_q_scale, L0_ffn_k_scale, L0_ffn_Wo, L0_ffn_ln_g, L0_ffn_ln_b, L0_ffn_W1, L0_ffn_b1, L0_ffn_W2, L0_ffn_b2)
    return x

_drawn_inputs = setup_inputs


def setup_inputs(seed=0):
    import zlib

    import numpy as np

    out = dict(_drawn_inputs(seed))
    spreads = {'L0_attn_norm_w': (1.0, 0.2),
     'L0_attn_conv_b': (0.0, 0.1),
     'L0_attn_W_D': (1.0, 0.2),
     'L0_ffn_q_scale': (1.0, 0.2),
     'L0_ffn_k_scale': (1.0, 0.2),
     'L0_ffn_ln_g': (1.0, 0.2),
     'L0_ffn_ln_b': (0.0, 0.1),
     'L0_ffn_b1': (0.0, 0.1),
     'L0_ffn_b2': (0.0, 0.1)}
    factors = {}
    for name, (base, spread) in spreads.items():
        noise = np.random.default_rng([zlib.crc32(name.encode()), seed]).standard_normal(out[name].shape)
        drawn = base * np.exp(spread * noise) if base else spread * noise
        out[name] = jnp.asarray(drawn.astype(out[name].dtype))
    for name, factor in factors.items():
        out[name] = (out[name] * factor).astype(out[name].dtype)
    return out
```

```python
from contextlib import ExitStack

import numpy as np
import concourse.bass as bass
from concourse import mybir

F32 = mybir.dt.float32
BF16 = mybir.dt.bfloat16
ALU = mybir.AluOpType
ACT = mybir.ActivationFunctionType
AX = mybir.AxisListType

P = 128
B, L, D = 2, 1024, 128
T = B * L
TILES = T // P
CH = 512
NCH = T // CH
E, N, DDELTA, DCONV = 256, 16, 64, 4
HALVES = E // P
EPS = 1e-5
DEPTH, HEADS, DH, WIN = 6, 16, 64, 32
INNER = HEADS * DH
PAIRS = HEADS // 2
STEP = 256
STEPS = T // STEP
PER_LAYER = PAIRS * STEPS
DI = int(D * 4 * 2 / 3)
MT = [(0, 128), (128, 128), (256, DI - 256)]
PAD = WIN
NEG = -1e30
NVEC = 9


def wait(eng, sem, value):
    if isinstance(value, int) and value <= 0:
        return
    eng.wait_ge(sem, value)


def stand(eng, sem):
    eng.sem_inc(sem, 1)


def bcast_last(ap, n):
    return ap.unsqueeze(len(ap.shape)).to_broadcast(list(ap.shape) + [n])


def mamba_block(nc, d, keep):
    with ExitStack() as ctx:
        def sb(name, shape, dt=F32):
            return ctx.enter_context(nc.sbuf_tensor(name, shape, dt))

        def sem(name):
            return ctx.enter_context(nc.semaphore(name))

        XT, XRES, XS, MOD, ident, ones, epsc = (keep[k] for k in ("XT", "XRES", "XS", "MOD", "ident", "ones", "epsc"))
        ps = keep["ps"]

        x_in = sb("x_in", [P, TILES, D])
        H1 = sb("H1", [P, T])
        XN = sb("XN", [P, T])
        scr = sb("scr", [P, 10, L])
        XP = sb("XP", [P, HALVES, B, L + DCONV - 1])
        XC = sb("XC", [P, HALVES, T])
        DL = sb("DL", [P, HALVES, T])
        U = sb("U", [P, HALVES, T])
        SK = sb("SK", [P, HALVES, T])
        T1 = sb("T1", [DDELTA, T])
        mid_t = sb("mid_t", [2 * N, T], BF16)
        BCS = sb("BCS", [6 * N, T], BF16)
        SEL = sb("SEL", [6 * N, 2 * N, P], BF16)
        w_in = sb("w_in", [P, E])
        w_skip = sb("w_skip", [P, E])
        w_cat = sb("w_cat", [P, HALVES, DDELTA + 2 * N])
        w_d2 = sb("w_d2", [DDELTA, E])
        w_out = sb("w_out", [P, HALVES, D])
        w_mod = sb("w_mod", [P, 6 * D])
        cT = sb("cT", [P, B])
        cols = sb("cols", [P, HALVES, 3 + DCONV])
        norm_w = sb("norm_w", [P, 1])
        a_log = sb("a_log", [P, HALVES, N])
        a_neg = sb("a_neg", [P, HALVES, N])
        gtmp = sb("gtmp", [P, 2, 2, B])

        flat = scr[:].rearrange("p a b -> p (a b)")

        def role(k, c):
            return flat[:, (k * NCH + c) * CH:(k * NCH + c + 1) * CH]

        BCF = U[0:2 * N, 0, :]
        R1 = U[0:2 * N, 1, :]
        AE = [scr[:, 0, :], scr[:, 1, :]]
        BB = [scr[:, 2, :], scr[:, 3, :]]
        DU = [scr[:, 4, :], scr[:, 5, :]]
        HS = [scr[:, 6, :], scr[:, 7, :]]
        HC = [scr[:, 8, :], scr[:, 9, :]]

        ld_x, ld_w = sem("ld_x"), sem("ld_w")
        s_sel, s_const, s_id0, s_id, s_pads = sem("s_sel"), sem("s_const"), sem("s_id0"), sem("s_id"), sem("s_pads")
        s_silu_c, s_mod, s_mod_sb, s_modf = sem("s_silu_c"), sem("s_mod"), sem("s_mod_sb"), sem("s_modf")
        s_xtp, s_xt = sem("s_xtp"), sem("s_xt")
        mean_ps, cen, sq, var_ps, std, rstd, z, hh = (sem("n_" + k) for k in
                                                      ("mean_ps", "cen", "sq", "var_ps", "std", "rstd", "z", "h"))
        r_sq, r_ps, r_std, r_rstd, xn = (sem("r_" + k) for k in ("sq", "ps", "std", "rstd", "xn"))
        pj_ps, pj = sem("pj_ps"), sem("pj")
        conv, xc = sem("conv"), sem("xc")
        cat_ps, t1c, bcf, hi, r1, midc, lo = (sem(k) for k in ("cat_ps", "t1c", "bcf", "hi", "r1", "midc", "lo"))
        dl_ps, sp_abs, sp_exp, sp_ln, relu_d, delta, u_done = (
            sem(k) for k in ("dl_ps", "sp_abs", "sp_exp", "sp_ln", "relu_d", "delta", "u_done"))
        s_aexp, s_aneg = sem("s_aexp"), sem("s_aneg")
        b_ps, b_sb, c_ps, ae, du, scan, hc, yacc = (
            sem(k) for k in ("b_ps", "b_sb", "c_ps", "ae", "du", "scan", "hc", "yacc"))
        y_d, y_g, o_ps, o_h, x_new = (sem(k) for k in ("y_d", "y_g", "o_ps", "o_h", "x_new"))
        m2_ps, cen2, sq2, v2_ps, std2, rstd2, z2, h2 = (sem("m2_" + k) for k in
                                                        ("mean_ps", "cen", "sq", "var_ps", "std", "rstd", "z", "h"))
        kept, xs_ready = sem("kept"), sem("xs_ready")

        loads = [
            (w_mod[:], d["wmod"]), (cT[:], d["cT"]),
            (w_in[:], d["in_wT"]), (w_skip[:], d["skip_wT"]), (norm_w[:], d["norm_w"]),
            (cols[:], d["cols"]), (w_cat[:], d["w_cat"]), (w_d2[:], d["Wd2T"]), (a_log[:], d["A_log"]),
            (w_out[:], d["out_wT"]),
        ]
        all_w = 16 * len(loads)

        def chunk(t, c):
            return t[:, c * CH:(c + 1) * CH]

        def modcol(j, b):
            return MOD[:, j, b:b + 1]

        block = ctx.enter_context(nc.Block())

        @block.sync
        def _(sp):
            sp.dma_start(x_in[:], d["x"]).then_inc(ld_x, 16)
            for dst, src in loads:
                sp.dma_start(dst, src).then_inc(ld_w, 16)
            sp.wait_ge(ld_x, 16)
            sp.wait_ge(ld_w, all_w)

        @block.tensor
        def _(pe):
            def layer_norm(src_ready, mean_sem, cen_sem, sq_sem, var_sem, std_sem):
                for i in range(NCH + 1):
                    if i < NCH:
                        wait(pe, src_ready, i + 1)
                        wait(pe, cen_sem, i - 1)
                        nc.tensor.matmul(ps[:, 2 + i % 2, :], ones[:], chunk(XT, i),
                                         start=True, stop=True).then_inc(mean_sem, 1)
                    if i >= 1:
                        c = i - 1
                        wait(pe, sq_sem, c + 1)
                        wait(pe, std_sem, c - 1)
                        nc.tensor.matmul(ps[:, 4 + c % 2, :], ones[:], role(1, c),
                                         start=True, stop=True).then_inc(var_sem, 1)

            pe.wait_ge(s_id, 1)
            pe.wait_ge(ld_x, 16)
            for c in range(NCH):
                wait(pe, s_xt, c - 1)
                for k in range(CH // P):
                    mm = nc.tensor.transpose(ps[:, c % 2, k * P:(k + 1) * P], x_in[:, c * 4 + k, :], ident[:])
                mm.then_inc(s_xtp, 1)
            pe.wait_ge(ld_w, all_w)
            pe.wait_ge(s_silu_c, 1)
            for j in range(6):
                mm = nc.tensor.matmul(ps[:, 7, j * B:(j + 1) * B], w_mod[:, j * D:(j + 1) * D], cT[:],
                                      start=True, stop=True)
            mm.then_inc(s_mod, 1)
            pe.wait_ge(s_const, 1)
            layer_norm(s_xt, mean_ps, cen, sq, var_ps, std)
            pe.wait_ge(s_mod_sb, 1)
            for c in range(NCH):
                wait(pe, r_sq, c + 1)
                wait(pe, r_std, c - 1)
                nc.tensor.matmul(ps[:, 6 + c % 2, :], ones[:], role(1, c), start=True, stop=True).then_inc(r_ps, 1)
            for c in range(NCH):
                pe.wait_ge(xn, c + 1)
                for k in range(4):
                    q = 4 * c + k
                    if c < 2:
                        pe.wait_ge(xn, NCH)
                    wait(pe, pj, q - 7)
                    w = (w_in, w_skip)[k // 2]
                    nc.tensor.matmul(ps[:, q % 8, :], w[:, (k % 2) * P:(k % 2 + 1) * P], chunk(XN, c),
                                     start=True, stop=True).then_inc(pj_ps, 1)
            pe.wait_ge(pj, 4 * NCH)
            pe.wait_ge(xc, HALVES * B)
            for c in range(NCH):
                for h in range(HALVES):
                    mm = nc.tensor.matmul(ps[0:DDELTA + 2 * N, c, :], w_cat[:, h, :], chunk(XC[:, h, :], c),
                                          start=(h == 0), stop=(h == HALVES - 1))
                mm.then_inc(cat_ps, 1)
            for n in range(NCH * HALVES):
                c, h = n // 2, n % 2
                wait(pe, t1c, c + 1)
                wait(pe, relu_d, n - 3)
                wait(pe, sp_abs, n - 3)
                nc.tensor.matmul(ps[:, 4 + n % 4, :], w_d2[:, h * P:(h + 1) * P], chunk(T1, c),
                                 start=True, stop=True).then_inc(dl_ps, 1)

            def spread(row, bank, b):
                for k in range(2):
                    mm = nc.tensor.matmul(ps[:, bank + k, :], SEL[:, row, :],
                                          BCS[:, b * L + k * CH:b * L + (k + 1) * CH], start=True, stop=True)
                return mm

            def spread_b(b, n):
                wait(pe, b_sb, b * N + n)
                spread(n, 0, b).then_inc(b_ps, 1)

            def state(b, n, first=False, last=False):
                wait(pe, hc, (b * N + n) * HALVES)
                spread(n + N, 2, b).then_inc(c_ps, 1)
                if not last:
                    spread_b(b, n + 1)
                for h in range(HALVES):
                    pe.wait_ge(hc, (b * N + n) * HALVES + h + 1)
                    if first:
                        wait(pe, y_d, b * HALVES)
                    for k in range(2):
                        mm = nc.tensor.matmul(ps[:, 4 + 2 * h + k, :], ident[:], HC[h][:, k * CH:(k + 1) * CH],
                                              start=first, stop=last, skip_group_check=True)
                    mm.then_inc(yacc, 1)

            pe.wait_ge(lo, 1)
            pe.wait_ge(s_sel, 4)
            pe.wait_ge(sp_abs, NCH * HALVES)
            pe.wait_ge(relu_d, NCH * HALVES)
            for b in range(B):
                spread_b(b, 0)
                state(b, 0, first=True)
                with pe.Fori(1, N - 1) as n:
                    state(b, n)
                state(b, N - 1, last=True)
            for c in range(NCH):
                pe.wait_ge(y_g, 2 * (c // 2) + 2)
                if c == 0:
                    pe.wait_ge(y_g, 2 * B)
                for h in range(HALVES):
                    mm = nc.tensor.matmul(ps[:, c, :], w_out[:, h, :], chunk(XC[:, h, :], c),
                                          start=(h == 0), stop=(h == HALVES - 1))
                mm.then_inc(o_ps, 1)
            pe.wait_ge(x_new, NCH)
            layer_norm(x_new, m2_ps, cen2, sq2, v2_ps, std2)

        @block.scalar
        def _(act):
            def layer_norm(cen_sem, sq_sem, var_sem, std_sem):
                for i in range(NCH + 1):
                    if i < NCH:
                        act.wait_ge(cen_sem, i + 1)
                        nc.scalar.activation(role(1, i), role(0, i), ACT.Square).then_inc(sq_sem, 1)
                    if i >= 1:
                        c = i - 1
                        act.wait_ge(var_sem, c + 1)
                        nc.scalar.activation(role(2, c), ps[:, 4 + c % 2, :], ACT.Sqrt,
                                             bias=epsc[:]).then_inc(std_sem, 1)

            act.wait_ge(ld_w, all_w)
            nc.scalar.activation(cT[:], cT[:], ACT.Silu).then_inc(s_silu_c, 1)
            for c in range(NCH):
                act.wait_ge(s_xtp, c + 1)
                nc.scalar.copy(chunk(XT, c), ps[:, c % 2, :]).then_inc(s_xt, 1)
            act.wait_ge(s_const, 1)
            layer_norm(cen, sq, var_ps, std)
            for i in range(NCH + 1):
                if i < NCH:
                    act.wait_ge(hh, i + 1)
                    act.wait_ge(var_ps, i + 1)
                    nc.scalar.activation(role(1, i), chunk(H1, i), ACT.Square).then_inc(r_sq, 1)
                if i >= 1:
                    c = i - 1
                    act.wait_ge(r_ps, c + 1)
                    act.wait_ge(z, c + 1)
                    nc.scalar.activation(role(2, c), ps[:, 6 + c % 2, :], ACT.Sqrt,
                                         bias=epsc[:]).then_inc(r_std, 1)
            act.wait_ge(s_pads, 2)
            for q in range(4 * NCH):
                c, k = q // 4, q % 4
                act.wait_ge(pj_ps, q + 1)
                if k < 2:
                    dst = XP[:, k, c // 2, DCONV - 1 + (c % 2) * CH:DCONV - 1 + (c % 2 + 1) * CH]
                    nc.scalar.copy(dst, ps[:, q % 8, :]).then_inc(pj, 1)
                else:
                    nc.scalar.activation(chunk(SK[:, k - 2, :], c), ps[:, q % 8, :], ACT.Silu).then_inc(pj, 1)
            for n in range(HALVES * B):
                h, b = n % 2, n // 2
                act.wait_ge(conv, HALVES * B * (DCONV - 1) + n + 1)
                v = XC[:, h, b * L:(b + 1) * L]
                nc.scalar.activation(v, v, ACT.Silu).then_inc(xc, 1)
            nc.scalar.activation(a_neg[:], a_log[:], ACT.Exp).then_inc(s_aexp, 1)
            for c in range(NCH):
                act.wait_ge(cat_ps, c + 1)
                nc.scalar.copy(chunk(T1, c), ps[0:DDELTA, c, :]).then_inc(t1c, 1)
                nc.scalar.copy(chunk(BCF, c), ps[DDELTA:DDELTA + 2 * N, c, :]).then_inc(bcf, 1)
            NS = NCH * HALVES
            for n in range(NS):
                c, h = n // 2, n % 2
                act.wait_ge(dl_ps, n + 1)
                nc.scalar.activation(role(0, n), ps[:, 4 + n % 4, :], ACT.Abs, bias=cols[:, h, 1:2]).then_inc(sp_abs, 1)
            for n in range(NS):
                act.wait_ge(sp_abs, n + 1)
                nc.scalar.activation(role(0, n), role(0, n), ACT.Exp, scale=-1.0).then_inc(sp_exp, 1)
            for n in range(NS):
                act.wait_ge(sp_exp, n + 1)
                nc.scalar.activation(role(0, n), role(0, n), ACT.Ln, bias=1.0).then_inc(sp_ln, 1)

            def copy_b(b, n, par):
                act.wait_ge(b_ps, b * N + n + 1)
                wait(act, du, (b * N + n - 1) * HALVES)
                nc.scalar.copy(BB[par], ps[:, 0:2, :].rearrange("p a b -> p (a b)")).then_inc(b_sb, 1)

            def decay(b, n, h):
                t = (b * N + n) * HALVES + h
                wait(act, scan, t - 1)
                nc.scalar.activation(AE[h], DL[:, h, b * L:(b + 1) * L], ACT.Exp,
                                     scale=a_neg[:, h, bass.ds(n, 1)]).then_inc(ae, 1)

            act.wait_ge(delta, NS)
            act.wait_ge(u_done, HALVES)
            act.wait_ge(s_aneg, 1)
            for b in range(B):
                def two(m, b=b):
                    for dn in range(2):
                        copy_b(b, 2 * m + dn, dn)
                        for h in range(HALVES):
                            decay(b, 2 * m + dn, h)
                two(0)
                with act.Fori(1, N // 2) as m:
                    two(m)
            layer_norm(cen2, sq2, v2_ps, std2)
            for c in range(NCH):
                act.wait_ge(h2, c + 1)
                nc.scalar.copy(XS[0:D // 2, c // 2, PAD + (c % 2) * CH:PAD + (c % 2 + 1) * CH],
                               XT[0:D // 2, c * CH:(c + 1) * CH]).then_inc(xs_ready, 1)

        @block.vector
        def _(dve):
            def layer_norm(mean_sem, cen_sem, std_sem, rstd_sem, z_sem):
                for i in range(NCH + 2):
                    if i < NCH:
                        dve.wait_ge(mean_sem, i + 1)
                        nc.vector.tensor_tensor(role(0, i), chunk(XT, i), ps[:, 2 + i % 2, :],
                                                ALU.subtract).then_inc(cen_sem, 1)
                    if i >= 1 and i - 1 < NCH:
                        c = i - 1
                        dve.wait_ge(std_sem, c + 1)
                        nc.vector.reciprocal(role(2, c), role(2, c)).then_inc(rstd_sem, 1)
                        dve.wait_ge(rstd_sem, c + 1)
                        dve.wait_ge(cen_sem, c + 1)
                        nc.vector.tensor_tensor(role(3, c), role(0, c), role(2, c), ALU.mult).then_inc(z_sem, 1)

            dve.wait_ge(s_mod, 1)
            nc.vector.tensor_copy(MOD[:].rearrange("p j b -> p (j b)"), ps[:, 7, 0:6 * B]).then_inc(s_mod_sb, 1)
            dve.wait_ge(s_mod_sb, 1)
            for i, j in enumerate((1, 4)):
                nc.vector.tensor_scalar(MOD[:, j, :], MOD[:, j, :], 1.0, None, ALU.add).then_inc(s_modf, 1)
            for i, j in enumerate((2, 5)):
                nc.vector.tensor_scalar(gtmp[:, i, 0, :], MOD[:, j, :], 0.0, 2.0, ALU.is_ge, ALU.mult).then_inc(s_modf, 1)
                nc.vector.scalar_tensor_tensor(gtmp[:, i, 1, :], MOD[:, j, :], -1.0, MOD[:, j, :],
                                               ALU.mult, ALU.max).then_inc(s_modf, 1)
            dve.wait_ge(s_modf, 6)
            nc.vector.tensor_scalar(gtmp[:, :, 1, :], gtmp[:, :, 1, :], 0.25, None, ALU.max).then_inc(s_modf, 1)
            dve.wait_ge(s_modf, 7)
            for i, j in enumerate((2, 5)):
                nc.vector.scalar_tensor_tensor(MOD[:, j, :], gtmp[:, i, 0, :], -1.0, gtmp[:, i, 1, :],
                                               ALU.add, ALU.mult).then_inc(s_modf, 1)
            layer_norm(mean_ps, cen, std, rstd, z)
            for c in range(NCH):
                dve.wait_ge(r_std, c + 1)
                nc.vector.reciprocal(role(2, c), role(2, c)).then_inc(r_rstd, 1)
                dve.wait_ge(r_rstd, c + 1)
                dve.wait_ge(hh, c + 1)
                nc.vector.scalar_tensor_tensor(chunk(XN, c), chunk(H1, c), norm_w[:, 0:1], role(2, c),
                                               ALU.mult, ALU.mult).then_inc(xn, 1)
            G = HALVES * B
            for k in range(DCONV):
                for n in range(G):
                    h, b = n % 2, n // 2
                    o = XC[:, h, b * L:(b + 1) * L]
                    tap = DCONV - 1 - k
                    src = XP[:, h, b, tap:tap + L]
                    w = cols[:, h, 3 + tap:4 + tap]
                    if k == 0:
                        dve.wait_ge(pj, 4 * (2 * b + 2))
                        dve.wait_ge(s_pads, 2)
                        nc.vector.tensor_scalar(o, src, w, cols[:, h, 0:1], ALU.mult, ALU.add).then_inc(conv, 1)
                    else:
                        dve.wait_ge(conv, G * (k - 1) + n + 1)
                        nc.vector.scalar_tensor_tensor(o, src, w, o, ALU.mult, ALU.add).then_inc(conv, 1)
            dve.wait_ge(s_aexp, 1)
            nc.vector.tensor_scalar(a_neg[:], a_neg[:], -1.0, None, ALU.mult).then_inc(s_aneg, 1)
            dve.wait_ge(bcf, NCH)
            nc.vector.tensor_copy(BCS[0:2 * N, :], BCF).then_inc(hi, 1)
            dve.wait_ge(hi, 1)
            nc.vector.tensor_tensor(R1, BCF, BCS[0:2 * N, :], ALU.subtract).then_inc(r1, 1)
            dve.wait_ge(r1, 1)
            nc.vector.tensor_copy(mid_t[:], R1).then_inc(midc, 1)
            dve.wait_ge(midc, 1)
            nc.vector.tensor_copy(BCS[2 * N:4 * N, :], mid_t[:])
            nc.vector.tensor_tensor(BCS[4 * N:6 * N, :], R1, mid_t[:], ALU.subtract).then_inc(lo, 1)
            for n in range(NCH * HALVES):
                c, h = n // 2, n % 2
                dve.wait_ge(sp_abs, n + 1)
                nc.vector.tensor_scalar(chunk(DL[:, h, :], c), ps[:, 4 + n % 4, :], cols[:, h, 1:2], 0.0,
                                        ALU.add, ALU.max).then_inc(relu_d, 1)
            for n in range(NCH * HALVES):
                c, h = n // 2, n % 2
                dve.wait_ge(relu_d, n + 1)
                dve.wait_ge(sp_ln, n + 1)
                v = chunk(DL[:, h, :], c)
                nc.vector.tensor_tensor(v, v, role(0, n), ALU.add).then_inc(delta, 1)
            dve.wait_ge(delta, NCH * HALVES)
            dve.wait_ge(lo, 1)
            for h in range(HALVES):
                nc.vector.tensor_tensor(U[:, h, :], DL[:, h, :], XC[:, h, :], ALU.mult).then_inc(u_done, 1)

            def do_scan(b, n, h):
                t = (b * N + n) * HALVES + h
                dve.wait_ge(ae, t + 1)
                dve.wait_ge(du, t + 1)
                wait(dve, hc, t - 1)
                nc.vector.tensor_tensor_scan(HS[h], AE[h], DU[h], 0.0, ALU.mult, ALU.add).then_inc(scan, 1)

            def do_hc(b, n, h):
                t = (b * N + n) * HALVES + h
                dve.wait_ge(scan, t + 1)
                dve.wait_ge(c_ps, b * N + n + 1)
                wait(dve, yacc, t - 1)
                nc.vector.tensor_tensor(HC[h], HS[h], ps[:, 2:4, :].rearrange("p a b -> p (a b)"),
                                        ALU.mult).then_inc(hc, 1)

            for b in range(B):
                def one(n, b=b):
                    do_scan(b, n, 1)
                    do_hc(b, n, 0)
                    do_scan(b, n + 1, 0)
                    do_hc(b, n, 1)

                do_scan(b, 0, 0)
                one(0)
                with dve.Fori(1, N - 1) as n:
                    one(n)
                do_scan(b, N - 1, 1)
                do_hc(b, N - 1, 0)
                do_hc(b, N - 1, 1)
                for h in range(HALVES):
                    dve.wait_ge(yacc, (b + 1) * N * HALVES - 1 + h)
                    v = XC[:, h, b * L:(b + 1) * L]
                    nc.vector.scalar_tensor_tensor(v, v, cols[:, h, 2:3],
                                                   ps[:, 4 + 2 * h:6 + 2 * h, :].rearrange("p a b -> p (a b)"),
                                                   ALU.mult, ALU.add).then_inc(y_d, 1)
            for c in range(NCH):
                dve.wait_ge(o_ps, c + 1)
                nc.vector.tensor_tensor(chunk(H1, c), chunk(H1, c), ps[:, c, :], ALU.add).then_inc(o_h, 1)
                dve.wait_ge(o_h, c + 1)
                nc.vector.scalar_tensor_tensor(chunk(XT, c), chunk(H1, c), modcol(2, c // 2), chunk(XT, c),
                                               ALU.mult, ALU.add).then_inc(x_new, 1)
            dve.wait_ge(x_new, NCH)
            layer_norm(m2_ps, cen2, std2, rstd2, z2)
            dve.wait_ge(s_pads, 2)
            for c in range(NCH):
                dve.wait_ge(h2, c + 1)
                n = CH - c % 2
                nc.vector.tensor_copy(XS[D // 2:D, c // 2, PAD + 1 + (c % 2) * CH:PAD + 1 + (c % 2) * CH + n],
                                      XT[D // 2:D, c * CH:c * CH + n]).then_inc(xs_ready, 1)

        @block.gpsimd
        def _(pool):
            nc.gpsimd.memset(ident[:], 0.0).then_inc(s_id0, 1)
            pool.wait_ge(s_id0, 1)
            nc.gpsimd.affine_select(out=ident[:], in_=ident[:], compare_op=ALU.not_equal, fill=1.0, base=0,
                                    pattern=[[-1, P]], channel_multiplier=1).then_inc(s_id, 1)
            nc.gpsimd.memset(ones[:], 1.0 / D)
            nc.gpsimd.memset(epsc[:], EPS).then_inc(s_const, 1)
            nc.gpsimd.memset(XP[:, :, :, 0:DCONV - 1], 0.0).then_inc(s_pads, 1)
            nc.gpsimd.memset(XS[:, :, 0:PAD + 1], 0.0).then_inc(s_pads, 1)
            nc.gpsimd.memset(SEL[:], 0.0).then_inc(s_sel, 1)
            for k in range(3):
                pool.wait_ge(s_sel, k + 1)
                nc.gpsimd.affine_select(out=SEL[:], in_=SEL[:], compare_op=ALU.not_equal, fill=1.0, base=-2 * N * k,
                                        pattern=[[-1, 2 * N], [0, P]], channel_multiplier=1).then_inc(s_sel, 1)

            def modulate(z_sem, out, j_scale, j_shift, out_sem):
                for c in range(NCH):
                    pool.wait_ge(z_sem, c + 1)
                    nc.gpsimd.tensor_scalar(chunk(out, c), role(3, c), modcol(j_scale, c // 2), modcol(j_shift, c // 2),
                                            ALU.mult, ALU.add).then_inc(out_sem, 1)

            pool.wait_ge(s_modf, 9)
            modulate(z, H1, 1, 0, hh)

            def drive(b, n, par, h):
                t = (b * N + n) * HALVES + h
                pool.wait_ge(b_sb, b * N + n + 1)
                wait(pool, scan, t - 1)
                nc.gpsimd.tensor_tensor(DU[h], U[:, h, b * L:(b + 1) * L], BB[par], ALU.mult).then_inc(du, 1)

            def gate(b, h):
                pool.wait_ge(y_d, b * HALVES + h + 1)
                v = XC[:, h, b * L:(b + 1) * L]
                nc.gpsimd.tensor_tensor(v, v, SK[:, h, b * L:(b + 1) * L], ALU.mult).then_inc(y_g, 1)

            for b in range(B):
                def two(m, b=b):
                    for dn in range(2):
                        for h in range(HALVES):
                            drive(b, 2 * m + dn, dn, h)
                if b > 0:
                    for h in range(HALVES):
                        gate(b - 1, h)

                pool.wait_ge(u_done, HALVES)
                two(0)
                with pool.Fori(1, N // 2) as m:
                    two(m)
            for h in range(HALVES):
                gate(B - 1, h)
            for c in range(NCH):
                pool.wait_ge(x_new, c + 1)
                nc.gpsimd.tensor_copy(chunk(XRES, c), chunk(XT, c)).then_inc(kept, 1)
            pool.wait_ge(kept, NCH)
            pool.wait_ge(cen2, NCH)
            modulate(z2, XT, 4, 3, h2)


def transformer_block(nc, d, keep):
    with ExitStack() as ctx:
        def sb(name, shape, dt=F32):
            return ctx.enter_context(nc.sbuf_tensor(name, shape, dt))

        def sem(name):
            return ctx.enter_context(nc.semaphore(name))

        XT, XRES, XS, MOD, ident, ones, epsc = (keep[k] for k in ("XT", "XRES", "XS", "MOD", "ident", "ones", "epsc"))
        ps = keep["ps"]

        W = sb("W", [P, PAIRS, 3, P])
        WO = sb("WO", [P, PAIRS, D])
        W1 = sb("W1", [P, 2 * DI])
        W2 = sb("W2", [P, 3, D])
        VEC = sb("VEC", [P, NVEC, DEPTH])
        CUR = sb("CUR", [P, NVEC])
        QKS = sb("QKS", [P, DEPTH, 2, DH])
        QK4 = sb("QK4", [P, 2, 2, DH])
        TC = sb("TC", [P, L // P, 2 * P])
        TS = sb("TS", [P, L // P, 2 * P])
        MASK = sb("MASK", [P, 2, 2, P])
        mhalf = sb("mhalf", [P, 8])
        QKT = sb("QKT", [P, 2, B, PAD + L])
        V = sb("V", [P, TILES, 4, DH + 1])
        OT = sb("OT", [P, NCH, PAIRS, CH])
        RAW = sb("RAW", [P, 2, 8, DH])
        SQ = sb("SQ", [P, 2, 8, DH])
        PC = sb("PC", [P, 2, 8, DH])
        PS = sb("PS", [P, 2, 8, DH])
        QK = sb("QK", [P, 2, 8, DH])
        SS = sb("SS", [P, 2, 8])
        RN = sb("RN", [P, 2, 8])
        SM = sb("SM", [P, 2, 4, DH])
        MX = sb("MX", [P, 2, 4])
        PR = sb("PR", [P, 2, 2, P])
        PT = sb("PT", [P, 2, 2, P])
        RC = sb("RC", [P, 2, 4])
        ON = sb("ON", [P, 2, 4, DH])
        OUT = sb("OUT", [P, TILES, D])

        ld_c = sem("ld_c")
        w_qkv, w_tab, w_o, w_1, w_2 = (sem(k) for k in ("w_qkv", "w_tab", "w_o", "w_1", "w_2"))
        (qkv_ps, raw, sq, v_cp, ss, prods, ssm, rn, rot, qk, qkT_ps, qkT, s_ps, sm, mx, sub, pr, pT_ps, pT, o_ps,
         rc, on, oT_ps, oT) = (sem("a_" + k) for k in (
             "qkv_ps", "raw", "sq", "v_cp", "ss", "prods", "ssm", "rn", "rot", "qk", "qkT_ps", "qkT", "s_ps", "sm",
             "mx", "sub", "pr", "pT_ps", "pT", "o_ps", "rc", "on", "oT_ps", "oT"))
        (cur, q4, tabs, wo_ps, x1, xs_top, xs_bot, mean_ps, cen, fsq, var_ps, std, rstd, z, xg, w1_ps, gel, hid,
         w2_ps, x2, ns_top, ns_bot) = (sem("f_" + k) for k in (
             "cur", "q4", "tabs", "wo_ps", "x1", "xs_top", "xs_bot", "mean_ps", "cen", "sq", "var_ps", "std",
             "rstd", "z", "xg", "w1_ps", "gel", "hid", "w2_ps", "x2", "ns_top", "ns_bot"))
        fin, fT_ps, fcp, stored = (sem(k) for k in ("fin", "fT_ps", "fcp", "stored"))
        paced_pe = sem("paced_pe")
        s_ones, s_mh, s_vz = sem("s_ones"), sem("s_mh"), sem("s_vz")

        NCONST = 5 + 3
        qkv_dram = d["Wqkv"].rearrange("l p (t i m) -> l p i t m", t=3, i=PAIRS)
        wo_dram = d["Wo"].rearrange("l (i p) m -> l p i m", p=P)

        def tokens(c):
            return slice(c * CH, (c + 1) * CH)

        def xs_cols(c):
            return XS[:, c // 2, PAD + (c % 2) * CH:PAD + (c % 2 + 1) * CH]

        def scratch(c, k):
            return OT[:, c, k, :]

        block = ctx.enter_context(nc.Block())

        @block.sync
        def _(sp):
            sp.wait_ge(s_vz, 1)
            sp.dma_start(VEC[:, 0:3, :], d["vec3"]).then_inc(ld_c, 16)
            for part in range(2):
                for m, (lo_, size) in enumerate(MT):
                    sp.dma_start(VEC[0:size, 3 + 3 * part + m, :],
                                 d["b1T"][part * DI + lo_:part * DI + lo_ + size, :]).then_inc(ld_c, 16)
            sp.dma_start(QKS[:], d["qks"]).then_inc(ld_c, 16)
            sp.dma_start(MASK[:].rearrange("p a b c -> p (a b c)"), d["mask"]).then_inc(ld_c, 16)

            def load_pair(l, i):
                sp.dma_start(W[:, i, :, :], qkv_dram[l, :, i]).then_inc(w_qkv, 16)

            def load_tables():
                sp.dma_start(TC[:], d["tcos"]).then_inc(w_tab, 16)
                sp.dma_start(TS[:], d["tsin"]).then_inc(w_tab, 16)

            def load_w1(l):
                sp.dma_start(W1[:], d["W1"][l]).then_inc(w_1, 16)

            def load_w2(l):
                sp.dma_start(W2[:, 0:2, :], d["W2"][l, 0:256, :].rearrange("(k p) m -> p k m", p=P)).then_inc(w_2, 16)
                sp.dma_start(W2[0:DI - 256, 2, :], d["W2"][l, 256:DI, :]).then_inc(w_2, 16)

            load_tables()
            for i in range(PAIRS):
                load_pair(0, i)
            sp.dma_start(WO[:], wo_dram[0]).then_inc(w_o, 16)
            load_w1(0)
            load_w2(0)
            with sp.Fori(1, DEPTH) as l:
                with sp.Fori(0, PAIRS) as i:
                    sp.wait_ge(qkv_ps, (l - 1) * PER_LAYER + i * STEPS + STEPS)
                    load_pair(l, i)
                sp.wait_ge(prods, l * PER_LAYER)
                load_tables()
                sp.wait_ge(wo_ps, l * NCH)
                sp.dma_start(WO[:], wo_dram[l]).then_inc(w_o, 16)
                sp.wait_ge(w1_ps, l * NCH * 3)
                load_w1(l)
                sp.wait_ge(w2_ps, l * NCH)
                load_w2(l)
            for c in range(NCH):
                sp.wait_ge(fcp, c + 1)
                sp.dma_start(d["out"][:, 4 * c:4 * c + 4, :], OUT[:, 4 * c:4 * c + 4, :]).then_inc(stored, 16)
            sp.wait_ge(stored, 16 * NCH)
            sp.wait_ge(w_qkv, 16 * PAIRS * DEPTH)
            sp.wait_ge(w_tab, 32 * DEPTH)
            sp.wait_ge(w_o, 16 * DEPTH)
            sp.wait_ge(w_1, 16 * DEPTH)
            sp.wait_ge(w_2, 32 * DEPTH)


        class Step:
            def __init__(self, eng, l, i, s, lag, head, tail):
                self.eng, self.head = eng, head
                self.before = s - lag
                self.on = not (head and s < lag) and not (tail and s >= lag)
                self.s = (s - lag) % STEPS
                self.pair = i + (s - lag) // STEPS
                self.n = l * PER_LAYER + i * STEPS + (s - lag)
                self.par = (s - lag) % 2

            def made(self, sem):
                self.eng.wait_ge(sem, self.n + 1)

            def freed(self, sem, ago):
                if not (self.head and self.before < ago):
                    self.eng.wait_ge(sem, self.n - ago + 1)

        def layer_steps(eng, l, run):
            for s in range(STEPS):
                run(0, s, True, False)
            with eng.Fori(1, PAIRS) as i:
                for s in range(STEPS):
                    run(i, s, False, False)
            for s in range(4):
                run(PAIRS, s, False, True)

        def slot_quad(j):
            return (j % 4) // 2, (j // 4) * 2 + j % 2

        @block.tensor
        def _(pe):
            with pe.Fori(0, DEPTH) as l:
                def run(i, s, head, tail):
                    def at(lag):
                        return Step(pe, l, i, s, lag, head, tail)

                    t = at(0)
                    if t.on:
                        if s == 0 and head:
                            pe.wait_ge(w_qkv, 16 * PAIRS * (l + 1))
                            pe.wait_ge(ns_top, NCH * l + 1)
                            pe.wait_ge(ns_bot, NCH * l + 1)
                        t.freed(v_cp, 1)
                        b, j0 = s // 4, (s % 4) * STEP
                        wp = W[:, 0, :, :] if head else W[:, i, :, :]
                        for k in range(2):
                            c0 = PAD + j0 + k * P
                            nc.tensor.matmul(ps[:, k, 0:3 * P], XS[:, b, c0:c0 + P],
                                             wp.rearrange("p t m -> p (t m)"), start=True, stop=True)
                            mm = nc.tensor.matmul(ps[:, k, 3 * P:4 * P], XS[:, b, c0 - WIN:c0 - WIN + P],
                                                  wp[:, 2, :], start=True, stop=True)
                        mm.then_inc(qkv_ps, 1)
                    t = at(3)
                    if t.on:
                        t.made(pr)
                        at(4).freed(oT, 1)
                        for h in range(2):
                            mm = nc.tensor.transpose(ps[:, 3, h * P:(h + 1) * P], PR[:, t.par, h, :], ident[:])
                        mm.then_inc(pT_ps, 1)
                    t = at(2)
                    if t.on:
                        t.made(qkT)
                        t.freed(sm, 1)
                        stand(pe, paced_pe)
                        b, j0 = t.s // 4, (t.s % 4) * STEP
                        for h in range(2):
                            for j in range(8):
                                slot, quad = slot_quad(j)
                                c0 = PAD + j0 + j * WIN
                                o = slot * DH
                                mm = nc.tensor.matmul(ps[32 * quad:32 * quad + 32, 4 + h, o:o + DH],
                                                      QKT[DH * h:DH * h + DH, 0, b, c0:c0 + WIN],
                                                      QKT[DH * h:DH * h + DH, 1, b, c0 - WIN:c0 + WIN],
                                                      start=True, stop=True)
                        mm.then_inc(s_ps, 1)
                    av = at(3)

                    def values(slot):
                        for h in range(2):
                            for j in range(8):
                                if slot_quad(j)[0] != slot:
                                    continue
                                quad = slot_quad(j)[1]
                                r = slice(64 * slot, 64 * slot + 64)
                                q = j % 4
                                mm = nc.tensor.matmul(
                                    ps[32 * q:32 * q + 32, 6 + av.par, ((j // 4) * 2 + h) * (DH + 1):((j // 4) * 2 + h + 1) * (DH + 1)],
                                    PT[r, av.par, h, 32 * quad:32 * quad + 32],
                                    V[r, 2 * av.s + j // 4, 2 * (1 - j % 2) + h, :], start=True, stop=True)
                        return mm

                    if av.on:
                        if av.head and av.before == 0:
                            pe.wait_ge(s_ones, 2)
                        av.made(pT)
                        av.made(v_cp)
                        av.freed(on, 2)
                        stand(pe, paced_pe)
                        values(0)
                    t = at(1)
                    if t.on:
                        t.made(qk)
                        t.freed(qkT, 1)
                        for x in range(2):
                            for k in range(2):
                                src = QK[:, t.par, :, :].rearrange("p (k x h) d -> p k x (h d)", k=2, x=2)[:, k, x, :]
                                mm = nc.tensor.transpose(ps[:, 2, (x * 2 + k) * P:(x * 2 + k + 1) * P], src, ident[:])
                        mm.then_inc(qkT_ps, 1)
                    t = at(4)
                    if t.on:
                        t.made(on)
                        if tail:
                            t.freed(oT, 1)
                        for k in range(2):
                            src = ON[:, t.par, :, :].rearrange("p (k h) d -> p k (h d)", k=2)[:, k, :]
                            mm = nc.tensor.transpose(ps[:, 3, 2 * P + k * P:2 * P + (k + 1) * P], src, ident[:])
                        mm.then_inc(oT_ps, 1)
                    if av.on:
                        values(1).then_inc(o_ps, 1)

                layer_steps(pe, l, run)

                def out_proj(c):
                    if c == 0:
                        pe.wait_ge(w_o, 16 * (l + 1))
                        pe.wait_ge(oT, PER_LAYER * (l + 1))
                        pe.wait_ge(on, PER_LAYER * (l + 1))
                    if c >= 2:
                        pe.wait_ge(x1, NCH * l + c - 1)
                    for k in range(PAIRS):
                        mm = nc.tensor.matmul(ps[:, c % 2, :], WO[:, k, :], OT[:, c, k, :],
                                              start=(k == 0), stop=(k == PAIRS - 1))
                    mm.then_inc(wo_ps, 1)

                def mean(c):
                    pe.wait_ge(xs_top, NCH * l + c + 1)
                    pe.wait_ge(xs_bot, NCH * l + c + 1)
                    if c >= 1:
                        pe.wait_ge(cen, NCH * l + c)
                    nc.tensor.matmul(ps[:, 2, :], ones[:], xs_cols(c), start=True, stop=True).then_inc(mean_ps, 1)

                def var(c):
                    pe.wait_ge(fsq, NCH * l + c + 1)
                    if c >= 1:
                        pe.wait_ge(std, NCH * l + c)
                    nc.tensor.matmul(ps[:, 3, :], ones[:], scratch(c, 1), start=True, stop=True).then_inc(var_ps, 1)

                def up(c):
                    if c == 0:
                        pe.wait_ge(w_1, 16 * (l + 1))
                        pe.wait_ge(cur, l + 1)
                    pe.wait_ge(xg, NCH * l + c + 1)
                    for m, (m0, size) in enumerate(MT):
                        if 3 * c + m >= 2:
                            pe.wait_ge(hid, 3 * NCH * l + 3 * c + m - 1)
                        bank = (3 * c + m) % 2
                        nc.tensor.matmul(ps[0:size, 4 + bank, :], W1[:, m0:m0 + size], scratch(c, 3),
                                         start=True, stop=True)
                        nc.tensor.matmul(ps[0:size, 6 + bank, :], W1[:, DI + m0:DI + m0 + size], scratch(c, 3),
                                         start=True, stop=True).then_inc(w1_ps, 1)

                def down(c):
                    if c == 0:
                        pe.wait_ge(w_2, 32 * (l + 1))
                    if c >= 2:
                        pe.wait_ge(x2, NCH * l + c - 1)
                    pe.wait_ge(hid, 3 * NCH * l + 3 * c + 3)
                    for m, (m0, size) in enumerate(MT):
                        mm = nc.tensor.matmul(ps[:, c % 2, :], W2[0:size, m, :], scratch(c, 4 + m)[0:size, :],
                                              start=(m == 0), stop=(m == 2))
                    mm.then_inc(w2_ps, 1)

                out_proj(0)
                out_proj(1)
                mean(0)
                out_proj(2)
                var(0)
                mean(1)
                out_proj(3)
                var(1)
                mean(2)
                var(2)
                mean(3)
                var(3)
                up(0)
                up(1)
                down(0)
                up(2)
                down(1)
                up(3)
                down(2)
                down(3)
            for c in range(NCH):
                pe.wait_ge(fin, c + 1)
                for k in range(4):
                    mm = nc.tensor.transpose(ps[:, 4 + c, k * P:(k + 1) * P], XT[:, c * CH + k * P:c * CH + (k + 1) * P],
                                             ident[:])
                mm.then_inc(fT_ps, 1)

        @block.scalar
        def _(act):
            act.sem_inc(ns_top, 1)
            with act.Fori(0, DEPTH) as l:
                def run(i, s, head, tail):
                    def at(lag):
                        return Step(act, l, i, s, lag, head, tail)

                    qkv = ps[:, 0:2, :]
                    t = at(0)
                    if t.on:
                        t.made(qkv_ps)
                        t.freed(prods, 2)
                        nc.scalar.copy(RAW[:, t.par, :, :].rearrange("p (k a) d -> p k (a d)", k=2),
                                       qkv[:, :, 0:2 * P]).then_inc(raw, 1)
                    t = at(3)
                    if t.on:
                        t.made(pT_ps)
                        t.freed(o_ps, 2)
                        nc.scalar.copy(PT[:, t.par, :, :].rearrange("p h q -> p (h q)"),
                                       ps[:, 3, 0:2 * P]).then_inc(pT, 1)
                    t = at(0)
                    if t.on:
                        t.freed(o_ps, 8)
                        nc.scalar.copy(V[:, 2 * t.s:2 * t.s + 2, :, 0:DH],
                                       qkv[:, :, 2 * P:4 * P].rearrange("p k (a d) -> p k a d", d=DH)).then_inc(v_cp, 1)
                        t.made(raw)
                        t.freed(ss, 2)
                        nc.scalar.activation(SQ[:, t.par, :, :], RAW[:, t.par, :, :], ACT.Square).then_inc(sq, 1)
                    t = at(1)
                    if t.on:
                        t.made(qkT_ps)
                        t.freed(s_ps, 7)
                        b, c0 = t.s // 4, PAD + (t.s % 4) * STEP
                        nc.scalar.copy(QKT[:, :, b, c0:c0 + STEP],
                                       ps[:, 2, :].rearrange("p (x c) -> p x c", x=2)).then_inc(qkT, 1)
                    t = at(4)
                    if t.on:
                        t.made(oT_ps)
                        col = (t.s % 2) * STEP
                        nc.scalar.copy(OT[:, t.s // 2, t.pair, col:col + STEP], ps[:, 3, 2 * P:4 * P]).then_inc(oT, 1)
                    t = at(2)
                    if t.on:
                        t.made(sub)
                        t.freed(pT_ps, 2)
                        nc.scalar.activation(PR[:, t.par, :, :].rearrange("p h q -> p (h q)"),
                                             SM[:, t.par, :, :].rearrange("p a d -> p (a d)"), ACT.Exp).then_inc(pr, 1)

                layer_steps(act, l, run)

                def top(c, ready, made):
                    act.wait_ge(ready, NCH * l + c + 1)
                    nc.scalar.copy(xs_cols(c)[0:D // 2, :], XT[0:D // 2, tokens(c)]).then_inc(made, 1)

                def square(c):
                    act.wait_ge(cen, NCH * l + c + 1)
                    nc.scalar.activation(scratch(c, 1), scratch(c, 0), ACT.Square).then_inc(fsq, 1)

                def deviation(c):
                    act.wait_ge(var_ps, NCH * l + c + 1)
                    nc.scalar.activation(scratch(c, 2), ps[:, 3, :], ACT.Sqrt, bias=epsc[:]).then_inc(std, 1)

                def affine(c):
                    act.wait_ge(z, NCH * l + c + 1)
                    nc.scalar.activation(scratch(c, 3), scratch(c, 7), ACT.Identity, scale=CUR[:, 0:1],
                                         bias=CUR[:, 1:2]).then_inc(xg, 1)

                def gelu(c):
                    for m, (m0, size) in enumerate(MT):
                        act.wait_ge(w1_ps, 3 * NCH * l + 3 * c + m + 1)
                        dst = scratch(c, (7, 0, 1)[m])[0:size, :]
                        nc.scalar.activation(dst, ps[0:size, 6 + (3 * c + m) % 2, :], ACT.Gelu,
                                             bias=CUR[0:size, 6 + m:7 + m]).then_inc(gel, 1)

                top(0, x1, xs_top)
                top(1, x1, xs_top)
                square(0)
                top(2, x1, xs_top)
                deviation(0)
                square(1)
                top(3, x1, xs_top)
                deviation(1)
                act.wait_ge(cur, l + 1)
                affine(0)
                square(2)
                deviation(2)
                affine(1)
                square(3)
                deviation(3)
                affine(2)
                affine(3)
                gelu(0)
                gelu(1)
                top(0, x2, ns_top)
                gelu(2)
                top(1, x2, ns_top)
                gelu(3)
                top(2, x2, ns_top)
                top(3, x2, ns_top)
            for c in range(NCH):
                act.wait_ge(fT_ps, c + 1)
                nc.scalar.copy(OUT[:, 4 * c:4 * c + 4, :].rearrange("p k m -> p (k m)"), ps[:, 4 + c, :]).then_inc(fcp, 1)

        @block.vector
        def _(dve):
            dve.wait_ge(ld_c, 16 * 9)
            dve.sem_inc(ns_bot, 1)
            with dve.Fori(0, DEPTH) as l:
                dve.wait_ge(ns_bot, NCH * l + 1)
                nc.vector.tensor_copy(CUR[:], VEC[:, :, l]).then_inc(cur, 1)

                def run(i, s, head, tail):
                    def at(lag):
                        return Step(dve, l, i, s, lag, head, tail)

                    t = at(4)
                    if t.on:
                        t.made(o_ps)
                        o = ps[:, 6 + t.par, 0:4 * (DH + 1)].rearrange("p (a d) -> p a d", d=DH + 1)
                        t.freed(on, 2)
                        nc.vector.reciprocal(RC[:, t.par, :].unsqueeze(2), o[:, :, DH:DH + 1]).then_inc(rc, 1)
                        t.made(rc)
                        t.freed(oT_ps, 2)
                        nc.vector.tensor_tensor(ON[:, t.par, :, :], o[:, :, 0:DH],
                                                bcast_last(RC[:, t.par, :], DH), ALU.mult).then_inc(on, 1)
                    t = at(0)
                    if t.on:
                        if head and s == 0:
                            dve.wait_ge(tabs, 2 * (l + 1))
                        t.made(raw)
                        t.freed(rot, 2)
                        k0 = (s % 4) * 2
                        src = RAW[:, t.par, :, :].rearrange("p (k a) d -> p k (a d)", k=2)
                        nc.vector.tensor_tensor(PC[:, t.par, :, :].rearrange("p (k a) d -> p k (a d)", k=2), src,
                                                TC[:, k0:k0 + 2, :], ALU.mult)
                        t.made(sq)
                        t.freed(rn, 2)
                        nc.vector.tensor_reduce(SS[:, t.par, :], SQ[:, t.par, :, :], AX.X, ALU.add).then_inc(ss, 1)
                        nc.vector.tensor_tensor(PS[:, t.par, :, :].rearrange("p (k a) d -> p k (a d)", k=2), src,
                                                TS[:, k0:k0 + 2, :], ALU.mult).then_inc(prods, 1)
                        t.made(ss)
                        nc.vector.tensor_scalar(SS[:, t.par, :], SS[:, t.par, :], 1e-24, None, ALU.max).then_inc(ssm, 1)
                    t = at(2)
                    if t.on:
                        t.made(s_ps)
                        t.freed(pr, 2)
                        first = 1 if t.s % 4 == 0 else 0
                        nc.vector.scalar_tensor_tensor(
                            SM[:, t.par, :, :].rearrange("p (h a) d -> p h (a d)", h=2),
                            ps[:, 4:6, 0:P], float(np.sqrt(DH)), MASK[:, first, :, :],
                            ALU.mult, ALU.add).then_inc(sm, 1)
                        t.made(sm)
                        t.freed(sub, 2)
                        nc.vector.tensor_reduce(MX[:, t.par, :], SM[:, t.par, :, :], AX.X, ALU.max).then_inc(mx, 1)

                layer_steps(dve, l, run)

                def add_attn(c):
                    dve.wait_ge(wo_ps, NCH * l + c + 1)
                    nc.vector.tensor_tensor(XT[:, tokens(c)], XT[:, tokens(c)], ps[:, c % 2, :],
                                            ALU.add).then_inc(x1, 1)

                def late(c, ready, made):
                    dve.wait_ge(ready, NCH * l + c + 1)
                    n = CH - c % 2
                    nc.vector.tensor_copy(XS[D // 2:D, c // 2, PAD + 1 + (c % 2) * CH:PAD + 1 + (c % 2) * CH + n],
                                          XT[D // 2:D, c * CH:c * CH + n]).then_inc(made, 1)

                def centre(c):
                    dve.wait_ge(xs_top, NCH * l + c + 1)
                    dve.wait_ge(xs_bot, NCH * l + c + 1)
                    dve.wait_ge(mean_ps, NCH * l + c + 1)
                    nc.vector.tensor_tensor(scratch(c, 0), xs_cols(c), ps[:, 2, :], ALU.subtract).then_inc(cen, 1)

                def normal(c):
                    dve.wait_ge(std, NCH * l + c + 1)
                    nc.vector.reciprocal(scratch(c, 2), scratch(c, 2)).then_inc(rstd, 1)
                    dve.wait_ge(rstd, NCH * l + c + 1)
                    dve.wait_ge(cen, NCH * l + c + 1)
                    nc.vector.tensor_tensor(scratch(c, 7), scratch(c, 0), scratch(c, 2), ALU.mult).then_inc(z, 1)

                def hidden(c):
                    for m, (m0, size) in enumerate(MT):
                        dve.wait_ge(gel, 3 * NCH * l + 3 * c + m + 1)
                        nc.vector.scalar_tensor_tensor(
                            scratch(c, 4 + m)[0:size, :], ps[0:size, 4 + (3 * c + m) % 2, :], CUR[0:size, 3 + m:4 + m],
                            scratch(c, (7, 0, 1)[m])[0:size, :], ALU.add, ALU.mult).then_inc(hid, 1)

                def add_ffn(c):
                    dve.wait_ge(w2_ps, NCH * l + c + 1)
                    nc.vector.scalar_tensor_tensor(XT[:, tokens(c)], ps[:, c % 2, :], CUR[:, 2:3], XT[:, tokens(c)],
                                                   ALU.add, ALU.add).then_inc(x2, 1)

                add_attn(0)
                late(0, x1, xs_bot)
                add_attn(1)
                late(1, x1, xs_bot)
                centre(0)
                add_attn(2)
                late(2, x1, xs_bot)
                normal(0)
                centre(1)
                add_attn(3)
                late(3, x1, xs_bot)
                normal(1)
                centre(2)
                normal(2)
                centre(3)
                normal(3)
                dve.wait_ge(cur, l + 1)
                dve.wait_ge(xs_top, NCH * (l + 1))
                dve.wait_ge(xs_bot, NCH * (l + 1))
                hidden(0)
                hidden(1)
                add_ffn(0)
                late(0, x2, ns_bot)
                hidden(2)
                add_ffn(1)
                late(1, x2, ns_bot)
                hidden(3)
                add_ffn(2)
                late(2, x2, ns_bot)
                add_ffn(3)
                late(3, x2, ns_bot)
            for c in range(NCH):
                dve.wait_ge(ns_top, NCH * DEPTH + 1)
                dve.wait_ge(ns_bot, NCH * DEPTH + 1)
                nc.vector.scalar_tensor_tensor(XT[:, tokens(c)], XT[:, tokens(c)], MOD[:, 5, c // 2:c // 2 + 1],
                                               XRES[:, tokens(c)], ALU.mult, ALU.add).then_inc(fin, 1)

        @block.gpsimd
        def _(pool):
            nc.gpsimd.memset(VEC[:], 0.0).then_inc(s_vz, 1)
            nc.gpsimd.memset(V[:, :, :, DH:DH + 1], 1.0).then_inc(s_ones, 1)
            nc.gpsimd.memset(QKT[:, :, :, 0:PAD], 0.0).then_inc(s_ones, 1)
            nc.gpsimd.memset(mhalf[:], -0.5).then_inc(s_mh, 1)
            pool.wait_ge(s_mh, 1)
            pool.wait_ge(ld_c, 16 * 9)
            with pool.Fori(0, DEPTH) as l:
                for h in range(2):
                    ins = nc.gpsimd.tensor_copy(QK4[:, :, h, :], QKS[:, l, :, :])
                ins.then_inc(q4, 1)
                pool.wait_ge(q4, l + 1)
                pool.wait_ge(w_tab, 32 * (l + 1))
                for tab in (TC, TS):
                    nc.gpsimd.tensor_tensor(tab[:], tab[:],
                                            QK4[:].rearrange("p x h d -> p (x h d)").unsqueeze(1).to_broadcast([P, L // P, 2 * P]),
                                            ALU.mult).then_inc(tabs, 1)

                def run(i, s, head, tail):
                    def at(lag):
                        return Step(pool, l, i, s, lag, head, tail)

                    t = at(0)
                    if t.on:
                        t.made(ssm)
                        t.freed(qk, 2)
                        nc.gpsimd.tensor_tensor(RN[:, t.par, :], SS[:, t.par, :], mhalf[:], ALU.pow).then_inc(rn, 1)
                    t = at(2)
                    if t.on:
                        t.made(mx)
                        nc.gpsimd.tensor_tensor(SM[:, t.par, :, :], SM[:, t.par, :, :],
                                                bcast_last(MX[:, t.par, :], DH), ALU.subtract).then_inc(sub, 1)
                    t = at(0)
                    if t.on:
                        t.made(prods)
                        t.freed(qkT_ps, 2)
                        hd = DH // 2
                        nc.gpsimd.tensor_tensor(QK[:, t.par, :, 0:hd], PC[:, t.par, :, 0:hd], PS[:, t.par, :, hd:DH],
                                                ALU.add)
                        nc.gpsimd.tensor_tensor(QK[:, t.par, :, hd:DH], PC[:, t.par, :, hd:DH], PS[:, t.par, :, 0:hd],
                                                ALU.add).then_inc(rot, 1)
                        t.made(rot)
                        t.made(rn)
                        nc.gpsimd.tensor_tensor(QK[:, t.par, :, :], QK[:, t.par, :, :], bcast_last(RN[:, t.par, :], DH),
                                                ALU.mult).then_inc(qk, 1)

                layer_steps(pool, l, run)



def adaln_kernel(nc, d):
    with ExitStack() as ctx:
        def sb(name, shape, dt=F32):
            return ctx.enter_context(nc.sbuf_tensor(name, shape, dt))

        keep = {
            "XT": sb("XT", [P, T]),
            "XRES": sb("XRES", [P, T]),
            "XS": sb("XS", [P, B, PAD + L]),
            "MOD": sb("MOD", [P, 6, B]),
            "ident": sb("ident", [P, P]),
            "ones": sb("ones", [P, P]),
            "epsc": sb("epsc", [P, 1]),
            "ps": ctx.enter_context(nc.psum_tensor("ps", [P, 8, CH], F32)),
        }
        mamba_block(nc, d, keep)
        transformer_block(nc, d, keep)


def rotary_tables():
    half = np.arange(0, DH, 2, dtype=np.float32)
    inv_freq = (np.float32(1.0) / np.float32(10000.0) ** (half / np.float32(DH))).astype(np.float32)
    t = np.arange(L, dtype=np.float32)
    freqs = t[:, None] * inv_freq[None, :]
    base = ((half + np.float32(0.4 * DH)) / np.float32(1.4 * DH)).astype(np.float32)
    power = (t - L // 2) / (WIN // 2)
    scale = (base[None, :].astype(np.float64) ** power[:, None].astype(np.float64)).astype(np.float32)
    cos, sin = np.cos(freqs), np.sin(freqs)
    c2, s2 = np.concatenate([cos, cos], -1), np.concatenate([sin, -sin], -1)
    sc2 = np.concatenate([scale, scale], -1)
    out = []
    for tab in (c2, s2):
        qk = np.stack([tab * sc2, tab * (np.float32(1.0) / sc2)], 1)
        qk = np.repeat(qk[:, :, None, :], 2, axis=2).reshape(L // P, P, 4 * DH)
        out.append(np.ascontiguousarray(qk.transpose(1, 0, 2)).astype(np.float32))
    return out


def score_mask():
    q = np.arange(P)[:, None] % WIN
    c = np.arange(2 * WIN)[None, :]
    ok = (c >= q) & (c <= q + WIN)
    m = np.where(ok, 0.0, NEG).astype(np.float32)
    m = np.broadcast_to(m[:, None, None, None, :], (P, 2, 2, 2, 2 * WIN)).copy()
    m[0:WIN, 1, :, 0, 0:WIN] = NEG
    return m.reshape(P, -1)


def kernel(**inputs):
    import concourse.bacc as _bacc
    from concourse import mybir as _mybir
    from concourse.bass_utils import run_bass_kernel_spmd as _run

    nc = _bacc.Bacc("TRN2", target_bir_lowering=False, num_devices=1)
    arrays = {}

    def give(name, a):
        a = np.ascontiguousarray(a)
        arrays["in_" + name] = a
        return nc.dram_tensor("in_" + name, a.shape, _mybir.dt.from_np(a.dtype), kind="ExternalInput").ap()

    a = {k: np.asarray(v) for k, v in inputs.items()}
    m = {k[len("L0_attn_"):]: v for k, v in a.items() if k.startswith("L0_attn_")}
    f = {k[len("L0_ffn_"):]: v for k, v in a.items() if k.startswith("L0_ffn_")}
    tcos, tsin = rotary_tables()

    def halves(v):
        return v.reshape(HALVES, P, -1).transpose(1, 0, 2)

    d = {
        "x": give("x", m["resid"].reshape(TILES, P, D).transpose(1, 0, 2)),
        "wmod": give("wmod", a["L0_wmod"]),
        "cT": give("cT", a["L0_c"].T),
        "in_wT": give("in_wT", m["in_w"].T),
        "skip_wT": give("skip_wT", m["skip_w"].T),
        "norm_w": give("norm_w", m["norm_w"][:, None]),
        "cols": give("cols", np.concatenate([halves(m["conv_b"]), halves(m["Wd2_b"]), halves(m["W_D"]),
                                             halves(m["conv_w"])], 2)),
        "w_cat": give("w_cat", np.concatenate([halves(m["Wd1"].T), halves(m["WB"].T), halves(m["WC"].T)], 2)),
        "Wd2T": give("Wd2T", m["Wd2_w"].T),
        "A_log": give("A_log", halves(m["A_log"])),
        "out_wT": give("out_wT", halves(m["out_w"].T)),
        "Wqkv": give("Wqkv", f["Wqkv"]),
        "Wo": give("Wo", f["Wo"]),
        "W1": give("W1", f["W1"]),
        "W2": give("W2", f["W2"]),
        "vec3": give("vec3", np.stack([f["ln_g"].T, f["ln_b"].T, f["b2"].T], 1)),
        "b1T": give("b1T", f["b1"].T),
        "qks": give("qks", np.broadcast_to(np.stack([f["q_scale"], f["k_scale"]], 1)[None], (P, DEPTH, 2, DH))),
        "tcos": give("tcos", tcos),
        "tsin": give("tsin", tsin),
        "mask": give("mask", score_mask()),
    }
    d["out"] = nc.dram_tensor("out", (TILES, P, D), F32, kind="ExternalOutput").ap().rearrange("n p m -> p n m")
    adaln_kernel(nc, d)
    r = _run(nc, [arrays], core_ids=[0])
    return r.results[0]["out"].reshape(B, L, D)
```
